# Optimizing a Trainium2 kernel written in Bass

```python
import numpy as np
import jax
import jax.numpy as jnp

def _softmax(x, axis=-1):
    return jax.nn.softmax(x, axis=axis)

def _gelu(x):
    return jax.nn.gelu(x, approximate=True)

def _silu(x):
    return jax.nn.silu(x)

def _sigmoid(x):
    return jax.nn.sigmoid(x)

def _layernorm(x, axis=-1, eps=1e-05):
    m = jnp.mean(x, axis=axis, keepdims=True)
    v = jnp.var(x, axis=axis, keepdims=True)
    return (x - m) / jnp.sqrt(v + eps)

def _scatter_add(tgt, idx, src, axis=0):
    return tgt.at[idx].add(src)

def _segment_sum(src, seg, n):
    return jax.ops.segment_sum(src, seg, n)
kernel_name = 'mk_seq_postln_d1_jaxref_r4_5cb9ad'

def setup_inputs(seed: int=0):
    np.random.seed(seed)
    _w = jnp.asarray

    def _L0_attn_setup():
        import jax, jax.numpy as jnp
        import numpy as np
        B, S, E, H = (2, 512, 256, 16)
        D = E // H
        key = jax.random.key(seed)
        ks = jax.random.split(key, 8)
        hidden_states = jax.random.normal(ks[0], (B, S, E), dtype=jnp.float32)
        Wq = jax.random.normal(ks[1], (E, E), dtype=jnp.float32) * 0.02
        Wk = jax.random.normal(ks[2], (E, E), dtype=jnp.float32) * 0.02
        Wv = jax.random.normal(ks[3], (E, E), dtype=jnp.float32) * 0.02
        bq = jnp.zeros((E,), jnp.float32)
        bk = jnp.zeros((E,), jnp.float32)
        bv = jnp.zeros((E,), jnp.float32)
        eye = jnp.eye(E, dtype=jnp.float32)
        Wfq = eye + jax.random.normal(ks[4], (E, E), dtype=jnp.float32) * 0.02
        Wfk = eye + jax.random.normal(ks[5], (E, E), dtype=jnp.float32) * 0.02
        bfq = jnp.zeros((E,), jnp.float32)
        bfk = jnp.zeros((E,), jnp.float32)
        return dict(hidden_states=hidden_states, Wq=Wq, bq=bq, Wk=Wk, bk=bk, Wv=Wv, bv=bv, Wfq=Wfq, bfq=bfq, Wfk=Wfk, bfk=bfk)
    _L0_attn_in = _L0_attn_setup()

    def _L0_ffn_setup():
        import jax, jax.numpy as jnp
        import numpy as np
        B, S, D, T = (4, 1024, 256, 8)
        key = jax.random.key(seed)
        k1, k2, k3, k4 = jax.random.split(key, 4)
        x = jax.random.normal(k1, (B, S, D), dtype=jnp.float32)
        tile_sigs = jax.random.normal(k2, (T, D), dtype=jnp.float32)
        bound = 1.0 / np.sqrt(D)
        W = jax.random.uniform(k3, (T, D, D), minval=-bound, maxval=bound, dtype=jnp.float32)
        b = jax.random.uniform(k4, (T, D), minval=-bound, maxval=bound, dtype=jnp.float32)
        return {'x': x, 'tile_sigs': tile_sigs, 'W': W, 'b': b}
    _L0_ffn_in = _L0_ffn_setup()
    _d = {'L0_attn_hidden_states': _L0_attn_in['hidden_states'], 'L0_attn_Wq': _L0_attn_in['Wq'], 'L0_attn_bq': _L0_attn_in['bq'], 'L0_attn_Wk': _L0_attn_in['Wk'], 'L0_attn_bk': _L0_attn_in['bk'], 'L0_attn_Wv': _L0_attn_in['Wv'], 'L0_attn_bv': _L0_attn_in['bv'], 'L0_attn_Wfq': _L0_attn_in['Wfq'], 'L0_attn_bfq': _L0_attn_in['bfq'], 'L0_attn_Wfk': _L0_attn_in['Wfk'], 'L0_attn_bfk': _L0_attn_in['bfk'], 'L0_ffn_tile_sigs': _L0_ffn_in['tile_sigs'], 'L0_ffn_W': _L0_ffn_in['W'], 'L0_ffn_b': _L0_ffn_in['b']}
    _x0 = _d['L0_attn_hidden_states']
    _d['L0_attn_hidden_states'] = jax.random.normal(jax.random.fold_in(jax.random.key(seed), 1), (4, 1024, 256), dtype=_x0.dtype)
    del _x0
    return _d

def reference(L0_attn_hidden_states, L0_attn_Wq, L0_attn_bq, L0_attn_Wk, L0_attn_bk, L0_attn_Wv, L0_attn_bv, L0_attn_Wfq, L0_attn_bfq, L0_attn_Wfk, L0_attn_bfk, L0_ffn_tile_sigs, L0_ffn_W, L0_ffn_b):

    def _L0_attn_ref(hidden_states, Wq, bq, Wk, bk, Wv, bv, Wfq, bfq, Wfk, bfk):
        import jax, jax.numpy as jnp
        import numpy as np
        B, S, E, H = (2, 512, 256, 16)
        D = E // H
        b, s, e = hidden_states.shape
        d = e // H
        q = jax.nn.softmax((hidden_states @ Wq.T + bq) @ Wfq.T + bfq, axis=-1)
        k = jax.nn.softmax((hidden_states @ Wk.T + bk) @ Wfk.T + bfk, axis=-1)
        v = hidden_states @ Wv.T + bv
        split = lambda t: t.reshape(b, s, H, d).transpose(0, 2, 1, 3)
        q, k, v = (split(q), split(k), split(v))
        scores = jnp.einsum('bhsd,bhtd->bhst', q, k)
        probs = scores / jnp.sum(scores, axis=-1, keepdims=True)
        ctx = jnp.einsum('bhst,bhtd->bhsd', probs, v)
        return ctx.transpose(0, 2, 1, 3).reshape(b, s, e)

    def _L0_ffn_ref(x, tile_sigs, W, b):
        import jax, jax.numpy as jnp
        import numpy as np
        B, S, D, T = (4, 1024, 256, 8)
        scores = jnp.einsum('bsd,td->bst', x, jnp.sign(tile_sigs))
        idx = jnp.argmax(scores, axis=-1)
        all_out = jnp.einsum('bsd,tde->bste', x, W) + b[None, None]
        out = jnp.take_along_axis(all_out, idx[:, :, None, None], axis=2)
        return out[:, :, 0, :]
    x = L0_attn_hidden_states
    x = _layernorm(x + _L0_attn_ref(x, L0_attn_Wq, L0_attn_bq, L0_attn_Wk, L0_attn_bk, L0_attn_Wv, L0_attn_bv, L0_attn_Wfq, L0_attn_bfq, L0_attn_Wfk, L0_attn_bfk), axis=-1)
    x = _layernorm(x + _L0_ffn_ref(x, L0_ffn_tile_sigs, L0_ffn_W, L0_ffn_b), axis=-1)
    return x

_drawn_inputs = setup_inputs


def setup_inputs(seed=0):
    import zlib

    import numpy as np

    out = dict(_drawn_inputs(seed))
    spreads = {'L0_attn_bq': (0.0, 0.8),
     'L0_attn_bk': (0.0, 0.723),
     'L0_attn_bv': (0.0, 0.1),
     'L0_attn_bfq': (0.0, 0.414),
     'L0_attn_bfk': (0.0, 0.8)}
    factors = {'L0_attn_Wq': 3.13, 'L0_attn_Wfq': 3.15}
    for name, (base, spread) in spreads.items():
        noise = np.random.default_rng([zlib.crc32(name.encode()), seed]).standard_normal(out[name].shape)
        drawn = base * np.exp(spread * noise) if base else spread * noise
        out[name] = jnp.asarray(drawn.astype(out[name].dtype))
    for name, factor in factors.items():
        out[name] = (out[name] * factor).astype(out[name].dtype)
    return out
```

```python
from collections import namedtuple
from contextlib import ExitStack

import concourse.bass as bass
from concourse import mybir

F32 = mybir.dt.float32
F32R = mybir.dt.float32r
BF16 = mybir.dt.bfloat16
I32 = mybir.dt.int32
ALU = mybir.AluOpType
ACT = mybir.ActivationFunctionType
AX = mybir.AxisListType.X

P = 128
HEADS = 16
EPS = 1e-5
BODY = 8
GROUP = 4

Tile = namedtuple("Tile", "turn slot n least")


def tile_at(turn, turns, step, lag):
    d = step - lag
    assert -BODY <= d < BODY
    mine = turn if d >= 0 else turn - 1
    if isinstance(turn, int) and not 0 <= mine < turns:
        return None
    least_turn = mine if isinstance(turn, int) else (1 if d >= 0 else 0)
    slot = d % BODY
    return Tile(mine, slot, mine * BODY + slot, least_turn * BODY + slot)


def wait_tiles(engine, semaphore, tile, plus):
    if isinstance(tile.n, int) and tile.n + plus <= 0:
        return
    assert tile.least + plus >= 1 or isinstance(tile.n, int)
    engine.wait_ge(semaphore, tile.n + plus)


def wait_turns(engine, semaphore, tile, plus, each=1):
    if isinstance(tile.turn, int) and tile.turn + plus <= 0:
        return
    assert tile.least // BODY + plus >= 1 or isinstance(tile.n, int)
    engine.wait_ge(semaphore, (tile.turn + plus) * each)


def wait_groups(engine, semaphore, tile, plus, size=GROUP):
    n = tile.turn * (BODY // size) + tile.slot // size + plus
    if isinstance(n, int) and n <= 0:
        return
    assert tile.least // size + plus >= 1 or isinstance(tile.n, int)
    engine.wait_ge(semaphore, n)


def held(engine, turn, passed):
    if not isinstance(turn, int):
        engine.sem_inc(passed, 1)


def pipelined(engine, turns, body, after_first=None, drain=True):
    for step in range(BODY):
        body(0, step)
    if after_first:
        after_first()
    with engine.Fori(1, turns) as turn:
        for step in range(BODY):
            body(turn, step)
    for step in range(BODY if drain else 0):
        body(turns, step)


def build(nc, x, xT, Wq, Wk, WfqT, WfkT, WvT, bq, bk, bv, bfq, bfk, sigsT, W, b, out):
    N, E = x.shape
    X = W.shape[0]
    NT = N // P
    BATCHES = 4
    assert NT == BATCHES * BODY and E == 2 * P
    HW = E // HEADS
    HH = HEADS // 2
    KVW = P + HH
    ROW = E + 8
    REGION = N + P
    FILL = X * REGION
    TILES_B = -(-((N + X * (P - 1)) // P) // BODY) * BODY
    TURNS_B = TILES_B // BODY
    GROUPS = BODY // GROUP
    MM_LAG = 3
    RING = 4
    DEPTH = 3

    rows = nc.dram_tensor("routed_rows", (FILL + P, ROW), F32, kind="Internal").ap()

    with ExitStack() as ctx:
        def sb(name, shape, dt=F32):
            return ctx.enter_context(nc.sbuf_tensor(name, shape, dt))

        def sem(name):
            return ctx.enter_context(nc.semaphore(name))

        def sems(name, n):
            return [sem(f"{name}{i}") for i in range(n)]

        x_sb = sb("x_sb", [P, NT, E])
        w_sb = sb("w_sb", [P, 2, X * E])
        bias_sb = sb("bias_sb", [P, X * E])
        wkc = sb("wkc", [P, 2, 2, E], F32R)
        wqc = sb("wqc", [P, 2, E])
        wvT_sb = sb("wvT_sb", [P, 2, E])
        bk_row = sb("bk_row", [P, E])
        bq_row = sb("bq_row", [P, E])
        bv_row = sb("bv_row", [P, E])
        kvd = sb("kvd", [P, BATCHES, 2, KVW])
        sign = sb("sign", [P, 2, X])
        ident = sb("ident", [P, P])
        head_mask = sb("head_mask", [P, HH])
        before = sb("before", [P, P], BF16)
        ones = sb("ones", [P, P], BF16)
        eps = sb("eps", [P, 1])
        falling = sb("falling", [P, GROUP, X])
        region_start = sb("region_start", [P, GROUP, X])
        token_id = sb("token_id", [P, NT], I32)
        w_raw = sb("w_raw", [P, 4, 2, E])
        b_col = sb("b_col", [P, 2, 2])
        b_wide = sb("b_wide", [P, 2, 2, P])
        bf_row = sb("bf_row", [P, 2, E])
        sigs = sb("sigs", [P, 2, X])
        sign_neg = sb("sign_neg", [P, 2, X])
        iota_i = sb("iota_i", [P, 2 * X], I32)
        xT_sb = sb("xT_sb", [P, 2, 2, GROUP * P])
        xTs = sb("xTs", [P, GROUP, 2, 2, P], F32R)
        neg_s = sb("neg_s", [P, 2, E])
        neg_max = sb("neg_max", [P, 2])
        e_sb = sb("e_sb", [P, GROUP, E])
        zsum = sb("zsum", [P, 2])
        xr = sb("xr", [P, GROUP, E + 1])
        g_sb = sb("g_sb", [P, 2, E + 1])
        gT_sb = sb("gT_sb", [P, 2, E])
        kv_tmp = sb("kv_tmp", [P, 2, P])
        eT_sb = sb("eT_sb", [P, 2, 2, P])
        rden = sb("rden", [P, 2, 2, HH])
        ctxn = sb("ctxn", [P, 2, E])
        y = sb("y", [P, BODY, E])
        stats = sb("stats", [P, BODY, 6])
        mv = sb("mv", [P, BODY, 2])
        lnv = sb("lnv", [P, BODY])
        rstd = sb("rstd", [P, BODY])
        nmr = sb("nmr", [P, BODY])
        x1 = sb("x1", [P, BODY, ROW])
        x1T = sb("x1T", [P, GROUP, 2, P])
        best = sb("best", [P, GROUP])
        is_best = sb("is_best", [P, GROUP, X])
        first = sb("first", [P, GROUP])
        onehot = sb("onehot", [P, 2, GROUP + 1, X], BF16)
        at_row = sb("at_row", [P, GROUP, X])
        row_of = sb("row_of", [P, 2, GROUP], I32)
        count_i = sb("count_i", [P, X], I32)
        tiles_i = sb("tiles_i", [P, X], I32)
        tiles_f = sb("tiles_f", [P, X])
        ones_x = sb("ones_x", [P, X])
        tile_end = sb("tile_end", [P, X])
        skip_rows = sb("skip_rows", [P, X])
        iota_j = sb("iota_j", [P, TILES_B], I32)
        j_f = sb("j_f", [P, TILES_B])
        past = sb("past", [P, TILES_B, X])
        skipped = sb("skipped", [P, TILES_B, X])
        off_f = sb("off_f", [P, TILES_B])
        exp_f = sb("exp_f", [P, TILES_B])
        row_tab = sb("row_tab", [P, TILES_B], I32)
        expert = sb("expert", [P, TURNS_B + 1, BODY])
        packed = sb("packed", [P, TURNS_B + 1, BODY])
        place_value = sb("place_value", [P, BODY])
        packed_f = sb("packed_f", [P, TURNS_B + 1])
        expert_tab = sb("expert_tab", [P, TURNS_B + 1], I32)
        pad_tab = sb("pad_tab", [P, X], I32)
        filler = sb("filler", [P, ROW])
        xs = sb("xs", [P, BODY, ROW])
        xs_id = sb("xs_id", [P, TILES_B], I32)
        out_row = sb("out_row", [P, BODY], I32)
        xsT = sb("xsT", [P, RING, 2, P])
        o_sb = sb("o_sb", [P, BODY, E])

        assert X ** BODY <= 1 << 24

        bank = [ctx.enter_context(nc.psum_tensor(f"bank{i}", [P, 512], F32)) for i in range(8)]
        fold_ps, fold_row_ps = bank[2][:, :], bank[6][:, 0:E]
        proj_ps = [bank[0][:, 0:E], bank[1][:, 0:E]]
        g_ps = [bank[3][:, 0:E + 1], bank[4][:, 0:E + 1]]
        gT_ps = [bank[5][:, 0:E], bank[6][:, 0:E]]
        kv_ps = bank[7][:, 0:E].rearrange("p (h e) -> p h e", h=2)
        eT_ps = bank[2][:, 0:E].rearrange("p (c t) -> p c t", c=2)
        ctx_ps = [bank[3 + i][:, 0:2 * KVW].rearrange("p (h e) -> p h e", h=2) for i in range(2)]
        x1T_ps = bank[5][:, :].rearrange("p (t c n) -> p t c n", t=2, c=2)
        score_ps = bank[6][:, 0:GROUP * X].rearrange("p (t e) -> p t e", t=GROUP)
        rank_ps = bank[7][:, 0:GROUP * X].rearrange("p (t e) -> p t e", t=GROUP)
        f_ps = [bank[i][:, 0:E] for i in (0, 1, 6, 7)]
        xsT_ps = [bank[2 + i][:, 0:E].rearrange("p (c t) -> p c t", c=2) for i in range(RING)]
        count_ps = bank[7][:, 64:64 + X]

        wk_loaded, wq_loaded, wv_loaded = sem("wk_loaded"), sem("wq_loaded"), sem("wv_loaded")
        rest_loaded, wx_loaded, fill_stored = sem("rest_loaded"), sem("wx_loaded"), sem("fill_stored")
        ones_ready = sem("ones_ready")
        consts, consts_v, prep = sem("consts"), sem("consts_v"), sem("prep")
        wk_split, xTs_high, xTs_ready = sem("wk_split"), sem("xTs_high"), sem("xTs_ready")
        b_widened, fold_ready, fold_saved = sem("b_widened"), sem("fold_ready"), sem("fold_saved")
        sign_step, sign_ready, w_ready = sem("sign_step"), sem("sign_ready"), sem("w_ready")
        xT_loaded, x_loaded = sems("xT_loaded", 2), sems("x_loaded", 2)
        k_ready, k_neg, ek_ready, rz_ready = sem("k_ready"), sem("k_neg"), sem("ek_ready"), sem("rz_ready")
        xr_ready, g_done = sem("xr_ready"), sem("g_done")
        g_saved, gT_ready, gT_saved = sems("g_saved", 2), sem("gT_ready"), sems("gT_saved", 2)
        kv_ready, kv_biased, kvd_ready = sem("kv_ready"), sem("kv_biased"), sem("kvd_ready")
        q_ready, q_neg, eq_ready, eT_ready = sem("q_ready"), sem("q_neg"), sem("eq_ready"), sem("eT_ready")
        eT_saved, ctx_ready, rden_ready = sem("eT_saved"), sem("ctx_ready"), sem("rden_ready")
        ctxn_ready, y_ready, stats_ready = sem("ctxn_ready"), sem("y_ready"), sem("stats_ready")
        mv_ready, lnv_ready, rstd_ready = sem("mv_ready"), sem("lnv_ready"), sem("rstd_ready")
        nmr_ready, x1_ready, id_ready = sem("nmr_ready"), sem("x1_ready"), sem("id_ready")
        x1T_ready, x1T_saved, score_ready = sem("x1T_ready"), sem("x1T_saved"), sem("score_ready")
        best_ready, is_best_ready, ranked_best = sem("best_ready"), sem("is_best_ready"), sem("ranked_best")
        first_ready, onehot_ready, rank_ready = sem("first_ready"), sem("onehot_ready"), sem("rank_ready")
        at_row_ready, row_ready, carry_ready = sem("at_row_ready"), sem("row_ready"), sem("carry_ready")
        row_stored = sems("row_stored", BODY)
        count_ready, table_step, table_ready = sem("count_ready"), sem("table_step"), sem("table_ready")
        pads_ready, pads_stored = sem("pads_ready"), sem("pads_stored")
        xs_loaded, xsT_ready, xsT_saved = sems("xs_loaded", BODY), sem("xsT_ready"), sem("xsT_saved")
        f_ready, f_biased, f_stats = sem("f_ready"), sem("f_biased"), sem("f_stats")
        f_mv, f_lnv, f_rstd, f_nmr, f_normed = sem("f_mv"), sem("f_lnv"), sem("f_rstd"), sem("f_nmr"), sem("f_normed")
        out_stored = sems("out_stored", BODY)
        xs_id_saved, out_row_ready, o_free = sem("xs_id_saved"), sem("out_row_ready"), sem("o_free")
        dve_passed, pool_passed = sem("dve_passed"), sem("pool_passed")

        def halves(ap):
            return ap.rearrange("(c p) w -> p c w", c=2)

        def in_all(ap):
            return ap.rearrange("(o w) -> o w", o=1).to_broadcast([P, ap.shape[0]])

        def one(ap):
            return ap.rearrange("p o d -> p (o d)")

        def store_pads(engine, first):
            engine.wait_ge(pads_ready, 1)
            for e in range(first, X, 2):
                at = engine.value_load(pad_tab[0:1, e:e + 1], min_val=0, max_val=FILL)
                engine.dma_start(rows[bass.ds(at, P), :], filler[:, :]).then_inc(pads_stored, 16)

        def load_experts(engine, turn, step, packed):
            if step == 0:
                packed.clear()
                packed.append(engine.value_load(expert_tab[0:1, bass.ds(turn, 1)], min_val=0, max_val=X ** BODY - 1))

        def expert_columns(packed, step):
            bits = X.bit_length() - 1
            return bass.ds(((packed[0] >> (bits * step)) & (X - 1)) * E, E)

        block = ctx.enter_context(nc.Block())

        @block.sync
        def _(sp):
            def load_xT(batch, half):
                sp.dma_start(xT_sb[:, half, :, :],
                             halves(xT[:, bass.ds(batch * BODY * P + half * GROUP * P, GROUP * P)])
                             ).then_inc(xT_loaded[half], 16)

            def load_x(batch, half):
                sp.dma_start(x_sb[:, bass.ds(batch * BODY + half * GROUP, GROUP), :],
                             x[bass.ds((batch * BODY + half * GROUP) * P, GROUP * P), :]
                             .rearrange("(t p) e -> p t e", p=P)).then_inc(x_loaded[half], 16)

            sp.dma_start(w_raw[:, 0], halves(Wk)).then_inc(wk_loaded, 16)
            sp.dma_start(w_raw[:, 1], halves(WfkT)).then_inc(wk_loaded, 16)
            load_xT(0, 0)
            load_x(0, 0)
            load_xT(0, 1)
            load_x(0, 1)
            sp.dma_start(wvT_sb[:, :, :], halves(WvT)).then_inc(wv_loaded, 16)
            sp.dma_start(bv_row[:, :], in_all(bv)).then_inc(wv_loaded, 16)
            sp.dma_start(w_raw[:, 2], halves(Wq)).then_inc(wq_loaded, 16)
            sp.dma_start(w_raw[:, 3], halves(WfqT)).then_inc(wq_loaded, 16)
            sp.dma_start(b_col[:, 1], bq).then_inc(wq_loaded, 16)
            sp.dma_start(bf_row[:, 1], in_all(bfq)).then_inc(wq_loaded, 16)
            sp.dma_start(sigs[:, :, :], halves(sigsT)).then_inc(rest_loaded, 16)
            with sp.Fori(1, BATCHES) as batch:
                for half in range(2):
                    sp.wait_ge(xTs_ready, (batch - 1) * BODY + (half + 1) * GROUP)
                    load_xT(batch, half)
                    sp.wait_ge(xr_ready, (batch - 1) * BODY + (half + 1) * GROUP)
                    load_x(batch, half)
            for half in range(2):
                sp.wait_ge(xTs_ready, (BATCHES - 1) * BODY + (half + 1) * GROUP)
                load_xT(0, half)
            for c in range(2):
                sp.dma_start(w_sb[:, c, :].rearrange("p (x e) -> p x e", x=X),
                             W[:, c * P:(c + 1) * P, :].rearrange("x p e -> p x e")).then_inc(wx_loaded, 16)
            sp.dma_start(bias_sb[:, :], in_all(b.rearrange("x e -> (x e)"))).then_inc(wx_loaded, 16)
            with sp.Fori(1, BATCHES) as batch:
                for half in range(2):
                    sp.wait_ge(q_ready, (batch - 1) * BODY + (half + 1) * GROUP)
                    load_xT(batch, half)
            store_pads(sp, 0)
            sp.wait_ge(table_ready, 2)
            def first_rows(turn, group):
                return nc.values_load_multi_w_load_instructions(
                    row_tab[0:1, bass.ds(turn * BODY + group * GROUP, GROUP)],
                    engines=[mybir.EngineType.SP], min_val=0, max_val=FILL)[1]

            def load_rows(group, at):
                for i in range(GROUP):
                    slot = group * GROUP + i
                    sp.dma_start(xs[:, slot, :], rows[bass.ds(at[i], P), :]).then_inc(xs_loaded[slot], 16)

            at = [first_rows(0, group) for group in range(GROUPS)]
            sp.wait_ge(pads_stored, 16 * X)
            sp.wait_ge(fill_stored, 16)
            for slot in range(BODY):
                sp.wait_ge(row_stored[slot], 16 * BATCHES)
            for group in range(GROUPS):
                load_rows(group, at[group])
            with sp.Fori(1, TURNS_B) as turn:
                for group in range(GROUPS):
                    at = first_rows(turn, group)
                    sp.wait_ge(xs_id_saved, (turn - 1) * GROUPS + group + 1)
                    load_rows(group, at)
            for slot in range(BODY):
                sp.wait_ge(out_stored[slot], 16 * TURNS_B)

        @block.gpsimd
        def _(pool):
            pool.memset(ones[:, :], 1.0).then_inc(ones_ready, 1)
            pool.memset(ident[:, :], 0.0).then_inc(consts, 1)
            pool.memset(head_mask[:, :], 1.0).then_inc(consts, 1)
            pool.memset(before[:, :], 1.0).then_inc(consts, 1)
            pool.memset(filler[:, :], 0.0).then_inc(consts, 1)
            pool.memset(x1[:, :, E:ROW], 0.0).then_inc(consts, 1)
            pool.memset(eps[:, :], EPS).then_inc(consts, 1)
            pool.memset(ones_x[:, :], 1.0).then_inc(consts, 1)
            pool.memset(onehot[:, 0, GROUP, :], 0.0).then_inc(consts, 1)
            pool.memset(expert[:, :, :], 0.0).then_inc(consts, 1)
            for i in range(BODY):
                pool.memset(place_value[:, i:i + 1], float(X ** i)).then_inc(consts, 1)
            pool.iota(token_id[:, :], pattern=[[P, NT]], base=0, channel_multiplier=1).then_inc(consts, 1)
            pool.iota(iota_j[:, :], pattern=[[1, TILES_B]], base=0, channel_multiplier=0).then_inc(consts, 1)
            pool.iota(iota_i[:, 0:X], pattern=[[-1, X]], base=X, channel_multiplier=0).then_inc(consts, 1)
            pool.iota(iota_i[:, X:2 * X], pattern=[[REGION, X]], base=0, channel_multiplier=0).then_inc(consts, 1)
            pool.wait_ge(consts, 13 + BODY)
            pool.affine_select(out=ident[:, :], in_=ident[:, :], compare_op=ALU.not_equal, fill=1.0, base=0,
                               pattern=[[-1, P]], channel_multiplier=1).then_inc(consts_v, 1)
            pool.affine_select(out=before[:, :], in_=before[:, :], compare_op=ALU.is_ge, fill=0.0, base=-1,
                               pattern=[[1, P]], channel_multiplier=-1).then_inc(consts_v, 1)
            pool.affine_select(out=head_mask[:, :], in_=head_mask[:, :], compare_op=ALU.is_ge, fill=0.0, base=0,
                               pattern=[[-HW, HH]], channel_multiplier=1).then_inc(consts_v, 1)
            pool.iota(filler[:, E:E + 1].bitcast(I32), pattern=[[0, 1]], base=N,
                      channel_multiplier=0).then_inc(consts_v, 1)
            pool.wait_ge(consts_v, 4)
            pool.affine_select(out=head_mask[:, :], in_=head_mask[:, :], compare_op=ALU.is_ge, fill=0.0,
                               base=HW - 1, pattern=[[HW, HH]], channel_multiplier=-1).then_inc(consts_v, 1)
            pool.dma_start(rows[FILL:FILL + P, :], filler[:, :]).then_inc(fill_stored, 16)

            last_row, last_token = pool.to_reg(FILL + P - 1), pool.to_reg(N - 1)

            def put_ids(turn, slot):
                for i in range(2 if not isinstance(turn, int) or turn else 0):
                    pool.wait_ge(row_stored[slot + i], turn * 16)
                pool.tensor_copy(x1[:, slot:slot + 2, E].bitcast(I32),
                                 token_id[:, bass.ds(turn * BODY + slot, 2)]).then_inc(id_ready, 1)

            def scatter_x1(turn, is_last=False):
                for group in range(GROUPS):
                    pool.wait_ge(row_ready, turn * GROUPS + group + 1)
                    pool.wait_ge(x1_ready, turn * BODY + (group + 1) * GROUP)
                    pool.wait_ge(id_ready, (turn * GROUPS + group + 1) * 2)
                    held(pool, turn, pool_passed)
                    for i in range(GROUP):
                        slot = group * GROUP + i
                        pool.indirect_dma_start(
                            out=rows, out_offset=bass.IndirectOffsetOnAxis(ap=row_of[:, group, i:i + 1], axis=0),
                            in_=x1[:, slot, :], in_offset=None, bounds_check=last_row,
                            oob_is_err=False).then_inc(row_stored[slot], 16)
                    if not is_last:
                        put_ids(turn + 1, group * GROUP)
                        put_ids(turn + 1, group * GROUP + 2)

            pool.wait_ge(consts, 13 + BODY)
            for slot in range(0, BODY, 2):
                put_ids(0, slot)
            scatter_x1(0)
            with pool.Fori(1, BATCHES - 1) as turn:
                scatter_x1(turn)
            scatter_x1(BATCHES - 1, is_last=True)

            def scatter_out(turn):
                for slot in range(BODY):
                    if slot % GROUP == 0:
                        pool.wait_ge(xs_id_saved, turn * GROUPS + slot // GROUP + 1)
                        pool.tensor_copy(out_row[:, slot:slot + GROUP],
                                         xs_id[:, bass.ds(turn * BODY + slot, GROUP)]).then_inc(out_row_ready, 1)
                        pool.wait_ge(out_row_ready, turn * GROUPS + slot // GROUP + 1)
                    pool.wait_ge(f_normed, turn * BODY + slot + 1)
                    held(pool, turn, pool_passed)
                    pool.indirect_dma_start(
                        out=out, out_offset=bass.IndirectOffsetOnAxis(ap=out_row[:, slot:slot + 1], axis=0),
                        in_=o_sb[:, slot, :], in_offset=None, bounds_check=last_token,
                        oob_is_err=False).then_inc(out_stored[slot], 16)
                    if slot >= DEPTH:
                        pool.wait_ge(out_stored[slot - DEPTH], (turn + 1) * 16)
                        pool.sem_inc(o_free, 1)
                    elif not isinstance(turn, int):
                        pool.wait_ge(out_stored[slot - DEPTH], turn * 16)
                        pool.sem_inc(o_free, 1)

            pool.sem_inc(o_free, BODY)
            scatter_out(0)
            with pool.Fori(1, TURNS_B) as turn:
                scatter_out(turn)

        @block.scalar
        def _(act):
            act.dma_start(b_col[:, 0], bk).then_inc(wk_loaded, 16)
            act.dma_start(bf_row[:, 0], in_all(bfk)).then_inc(wk_loaded, 16)
            act.preload_act_table_set("natural_log_exp_and_others")

            def keys(turn, step):
                t = tile_at(turn, BATCHES, step, 2)
                if t is not None:
                    par = t.slot % 2
                    wait_tiles(act, k_neg, t, 1)
                    wait_tiles(act, g_done, t, 1 - GROUP)
                    act.activation(e_sb[:, t.slot % GROUP, :], neg_s[:, par, :], ACT.Exp, scale=-1.0,
                                   bias=neg_max[:, par:par + 1],
                                   accum_out=zsum[:, par:par + 1]).then_inc(ek_ready, 1)
                    if t.slot % GROUP == 0:
                        wait_turns(act, x_loaded[t.slot // GROUP], t, 1, 16)
                    wait_tiles(act, rz_ready, t, 1)
                    act.activation(xr[:, t.slot % GROUP, 0:E], one(x_sb[:, bass.ds(t.n, 1), :]), ACT.Copy,
                                   scale=xr[:, t.slot % GROUP, E:E + 1]).then_inc(xr_ready, 1)
                t = tile_at(turn, BATCHES, step, 4)
                if t is not None and t.slot == BODY - 1:
                    wait_tiles(act, g_done, t, 1)
                    act.copy(g_sb[:, 0, :], g_ps[0]).then_inc(g_saved[0], 1)
                t = tile_at(turn, BATCHES, step, 6)
                if t is not None and t.slot == BODY - 1:
                    wait_turns(act, gT_ready, t, 1)
                    act.copy(gT_sb[:, 0, :], gT_ps[0]).then_inc(gT_saved[0], 1)

            pipelined(act, BATCHES, keys, drain=False)
            keys(BATCHES, 0)
            keys(BATCHES, 1)

            def queries(turn, step):
                first_turn = isinstance(turn, int) and turn == 0
                if first_turn:
                    if step + 2 < BODY:
                        keys(BATCHES, step + 2)
                t = tile_at(turn, BATCHES, step, 1)
                if t is not None:
                    par = t.slot % 2
                    wait_tiles(act, eT_ready, t, 1)
                    wait_tiles(act, ctx_ready, t, -1)
                    act.copy(eT_sb[:, par], eT_ps).then_inc(eT_saved, 1)
                t = tile_at(turn, BATCHES, step, 0)
                if t is not None:
                    par = t.slot % 2
                    wait_tiles(act, q_neg, t, 1)
                    wait_tiles(act, eT_ready, t, 1 - GROUP)
                    if first_turn and step < GROUP:
                        act.wait_ge(g_done, NT - GROUP + 1 + step)
                    act.activation(e_sb[:, t.slot % GROUP, :], neg_s[:, par, :], ACT.Exp, scale=-1.0,
                                   bias=neg_max[:, par:par + 1]).then_inc(eq_ready, 1)
                for lag in (5, 4) if step % 2 == 1 else ():
                    t = tile_at(turn, BATCHES, step, lag)
                    if t is not None:
                        wait_groups(act, nmr_ready, t, 1, size=2)
                        wait_groups(act, id_ready, t, 1, size=2)
                        act.activation(x1[:, t.slot, 0:E], y[:, t.slot, :], ACT.Identity,
                                       scale=rstd[:, t.slot:t.slot + 1],
                                       bias=nmr[:, t.slot:t.slot + 1]).then_inc(x1_ready, 1)
                t = tile_at(turn, BATCHES, step, 4) if step % 2 == 0 else None
                if t is not None:
                    pair = slice(t.slot, t.slot + 2)
                    wait_groups(act, mv_ready, t, 1, size=2)
                    act.activation(lnv[:, pair], mv[:, pair, 1], ACT.Ln, bias=eps[:, 0:1]).then_inc(lnv_ready, 1)
                    wait_groups(act, lnv_ready, t, 1, size=2)
                    act.activation(rstd[:, pair], lnv[:, pair], ACT.Exp, scale=-0.5).then_inc(rstd_ready, 1)
                t = tile_at(turn, BATCHES, step, 6) if step % 2 == 0 else None
                if t is not None:
                    i = t.slot % GROUP
                    wait_tiles(act, x1T_ready, t, 2)
                    act.copy(x1T[:, i:i + 2], x1T_ps).then_inc(x1T_saved, 1)

            pipelined(act, BATCHES, queries)
            store_pads(act, 1)

            def experts(turn, step):
                t = tile_at(turn, TURNS_B, step, 0)
                if t is not None:
                    r = t.slot % RING
                    wait_tiles(act, xsT_ready, t, 1)
                    wait_tiles(act, f_ready, t, 1 - RING)
                    act.copy(xsT[:, r], xsT_ps[r]).then_inc(xsT_saved, 1)
                t = tile_at(turn, TURNS_B, step, 8)
                if t is not None:
                    wait_groups(act, f_nmr, t, 1, size=2)
                    wait_tiles(act, o_free, t, 1)
                    act.activation(o_sb[:, t.slot, :], y[:, t.slot, :], ACT.Identity,
                                   scale=rstd[:, t.slot:t.slot + 1],
                                   bias=nmr[:, t.slot:t.slot + 1]).then_inc(f_normed, 1)
                t = tile_at(turn, TURNS_B, step, 6) if step % 2 == 0 else None
                if t is not None:
                    pair = slice(t.slot, t.slot + 2)
                    wait_groups(act, f_mv, t, 1, size=2)
                    act.activation(lnv[:, pair], mv[:, pair, 1], ACT.Ln, bias=eps[:, 0:1]).then_inc(f_lnv, 1)
                    wait_groups(act, f_lnv, t, 1, size=2)
                    act.activation(rstd[:, pair], lnv[:, pair], ACT.Exp, scale=-0.5).then_inc(f_rstd, 1)
                if step % GROUP == GROUP - 1:
                    t = tile_at(turn, TURNS_B, step, GROUP - 1)
                    if t is not None:
                        act.copy(xs_id[:, bass.ds(t.n, GROUP)],
                                 xs[:, t.slot:t.slot + GROUP, E].bitcast(I32)).then_inc(xs_id_saved, 1)

            pipelined(act, TURNS_B, experts)

        @block.vector
        def _(dve):
            def widen(i, loaded):
                dve.wait_ge(loaded, 64)
                dve.tensor_copy(b_wide[:, i], b_col[:, i, :, None].to_broadcast([P, 2, P])).then_inc(b_widened, 1)

            def save_fold(i, wc, row):
                dve.wait_ge(fold_ready, 2 * i + 1)
                fold = fold_ps.rearrange("p (c f) -> p c f", c=2)
                if i:
                    dve.tensor_copy(wc[:, :, :], fold).then_inc(fold_saved, 1)
                else:
                    dve.tensor_copy(wc[:, 0], fold).then_inc(wk_split, 1)
                    dve.wait_ge(wk_split, 1)
                    dve.tensor_tensor(wc[:, 1], fold, wc[:, 0], ALU.subtract).then_inc(fold_saved, 1)
                dve.wait_ge(fold_ready, 2 * i + 2)
                dve.tensor_tensor(row[:, :], fold_row_ps, bf_row[:, i], ALU.add).then_inc(fold_saved, 1)

            widen(0, wk_loaded)

            def keys(turn, step):
                if isinstance(turn, int) and turn == 0 and step == 2:
                    save_fold(0, wkc, bk_row)
                t = tile_at(turn, BATCHES, step, 2)
                if t is not None:
                    par = t.slot % 2
                    wait_tiles(dve, k_ready, t, 1)
                    wait_tiles(dve, ek_ready, t, -1)
                    dve.wait_ge(fold_saved, 2)
                    held(dve, t.turn, dve_passed)
                    dve.tensor_tensor_reduce(neg_s[:, par, :], proj_ps[par], bk_row[:, :], -1.0, 3.0e38,
                                             ALU.add, ALU.min, neg_max[:, par:par + 1]).then_inc(k_neg, 1)
                t = tile_at(turn, BATCHES, step, 0)
                if t is not None:
                    ring = t.slot % GROUP
                    part = xT_sb[:, t.slot // GROUP, :, (t.slot % GROUP) * P:(t.slot % GROUP + 1) * P]
                    if t.slot % GROUP == 0:
                        wait_turns(dve, xT_loaded[t.slot // GROUP], t, 1, 16)
                    wait_tiles(dve, k_ready, t, 1 - GROUP)
                    dve.tensor_copy(xTs[:, ring, 0], part).then_inc(xTs_high, 1)
                    wait_tiles(dve, xTs_high, t, 1)
                    dve.tensor_tensor(xTs[:, ring, 1], part, xTs[:, ring, 0], ALU.subtract).then_inc(xTs_ready, 1)
                t = tile_at(turn, BATCHES, step, 2)
                if t is not None:
                    par = t.slot % 2
                    wait_tiles(dve, ek_ready, t, 1)
                    wait_tiles(dve, g_done, t, 1 - GROUP)
                    dve.reciprocal(xr[:, t.slot % GROUP, E:E + 1], zsum[:, par:par + 1]).then_inc(rz_ready, 1)
                t = tile_at(turn, BATCHES, step, 4)
                if t is not None and t.slot == BODY - 1:
                    wait_tiles(dve, g_done, t, 1)
                    dve.tensor_copy(g_sb[:, 1, :], g_ps[1]).then_inc(g_saved[1], 1)
                t = tile_at(turn, BATCHES, step, 6)
                if t is not None and t.slot == BODY - 1:
                    wait_turns(dve, gT_ready, t, 1)
                    dve.tensor_copy(gT_sb[:, 1, :], gT_ps[1]).then_inc(gT_saved[1], 1)
                t = tile_at(turn, BATCHES, step, 7)
                if t is not None and t.slot == BODY - 1:
                    wait_turns(dve, kv_ready, t, 1)
                    for h in range(2):
                        wait_turns(dve, g_saved[h], t, 1)
                    for h in range(2):
                        dve.scalar_tensor_tensor(out=kv_tmp[:, h, :], in0=bv_row[:, h * P:(h + 1) * P],
                                                 scalar=g_sb[:, h, E:E + 1], in1=kv_ps[:, h, :],
                                                 op0=ALU.mult, op1=ALU.add).then_inc(kv_biased, 1)
                        dve.tensor_scalar(one(kvd[:, bass.ds(t.turn, 1), h, P:KVW]), head_mask[:, :],
                                          g_sb[:, h, E:E + 1], None, ALU.mult).then_inc(kvd_ready, 1)
                    wait_turns(dve, kv_biased, t, 1, 2)
                    for h in range(2):
                        dve.tensor_tensor(
                            one(kvd[:, bass.ds(t.turn, 1), h, 0:P]).rearrange("p (h w) -> p h w", w=HW),
                            kv_tmp[:, h, :].rearrange("p (h w) -> p h w", w=HW),
                            head_mask[:, :, None].to_broadcast([P, HH, HW]), ALU.mult).then_inc(kvd_ready, 1)

            def queries_weights():
                dve.wait_ge(rest_loaded, 16)
                dve.tensor_scalar(sign_neg[:, :, :], sigs[:, :, :], 0.0, None, ALU.is_lt).then_inc(sign_step, 1)
                dve.wait_ge(sign_step, 1)
                dve.scalar_tensor_tensor(out=sign[:, :, :].rearrange("p c x -> p (c x)"),
                                         in0=sigs[:, :, :].rearrange("p c x -> p (c x)"), scalar=0.0,
                                         in1=sign_neg[:, :, :].rearrange("p c x -> p (c x)"), op0=ALU.is_gt,
                                         op1=ALU.subtract).then_inc(sign_ready, 1)
                widen(1, wq_loaded)
                save_fold(1, wqc, bq_row)
                dve.wait_ge(wv_loaded, 32)
                dve.wait_ge(consts, 13 + BODY)
                for i in range(GROUP):
                    dve.tensor_copy(falling[:, i, :], iota_i[:, 0:X])
                    last = dve.tensor_copy(region_start[:, i, :], iota_i[:, X:2 * X])
                last.then_inc(prep, 1)
                dve.tensor_copy(j_f[:, :], iota_j[:, :]).then_inc(prep, 1)

            dve.wait_ge(consts_v, 5)
            pipelined(dve, BATCHES, keys, after_first=queries_weights, drain=False)
            keys(BATCHES, 0)
            keys(BATCHES, 1)

            def expert_weights():
                dve.wait_ge(wx_loaded, 48)
                for c in range(2):
                    v = w_sb[:, c, :].rearrange("p (x e) -> p x e", x=X)[:, :, c * P:(c + 1) * P]
                    dve.tensor_tensor(v, v, ident[:, None, :].to_broadcast([P, X, P]), ALU.add).then_inc(w_ready, 1)

            def queries(turn, step):
                if isinstance(turn, int) and turn == 0:
                    if step + 2 < BODY:
                        keys(BATCHES, step + 2)
                front = tile_at(turn, BATCHES, step, 0)
                mid = tile_at(turn, BATCHES, step, 2)
                back = tile_at(turn, BATCHES, step, 3)
                small = []
                group = tile_at(turn, BATCHES, step, 10) if step % GROUP == 2 else None
                if group is not None:
                    small = route(group)
                group = tile_at(turn, BATCHES, step, 11) if step % GROUP == 3 else None
                if group is not None:
                    small = place(group)
                small = iter(small)

                next(small, None)
                if back is not None:
                    wait_tiles(dve, y_ready, back, 1)
                    dve.bn_stats(stats[:, back.slot, :], y[:, back.slot, :]).then_inc(stats_ready, 1)
                next(small, None)
                if mid is not None:
                    par = mid.slot % 2
                    wait_tiles(dve, ctx_ready, mid, 1)
                    dve.reciprocal(rden[:, par], ctx_ps[par][:, :, P:KVW]).then_inc(rden_ready, 1)
                next(small, None)
                t = tile_at(turn, BATCHES, step, 4) if step % 2 == 0 else None
                if t is not None:
                    wait_tiles(dve, stats_ready, t, 2)
                    held(dve, t.turn, dve_passed)
                    for i in range(2):
                        last = dve.bn_aggr(mv[:, t.slot + i, :], stats[:, t.slot + i, :])
                    last.then_inc(mv_ready, 1)
                next(small, None)
                if mid is not None:
                    par = mid.slot % 2
                    wait_tiles(dve, rden_ready, mid, 1)
                    dve.tensor_tensor(
                        ctxn[:, par, :].rearrange("p (h w) -> p h w", w=HW),
                        ctx_ps[par][:, :, 0:P].rearrange("p c (h w) -> p c h w", w=HW),
                        rden[:, par].rearrange("p c h -> p (c h)")[:, :, None].to_broadcast([P, HEADS, HW]),
                        ALU.mult).then_inc(ctxn_ready, 1)
                next(small, None)
                if front is not None:
                    par = front.slot % 2
                    wait_tiles(dve, q_ready, front, 1)
                    wait_tiles(dve, eq_ready, front, -1)
                    dve.wait_ge(fold_saved, 4)
                    held(dve, front.turn, dve_passed)
                    dve.tensor_tensor_reduce(neg_s[:, par, :], proj_ps[par], bq_row[:, :], -1.0, 3.0e38,
                                             ALU.add, ALU.min, neg_max[:, par:par + 1]).then_inc(q_neg, 1)
                t = tile_at(turn, BATCHES, step, 5) if step % 2 == 1 else None
                if t is not None:
                    pair = slice(t.slot, t.slot + 2)
                    wait_groups(dve, rstd_ready, t, 1, size=2)
                    dve.scalar_tensor_tensor(out=nmr[:, pair], in0=mv[:, pair, 0], scalar=-1.0,
                                             in1=rstd[:, pair], op0=ALU.mult, op1=ALU.mult).then_inc(nmr_ready, 1)
                next(small, None)
                if mid is not None:
                    wait_tiles(dve, ctxn_ready, mid, 1)
                    wait_tiles(dve, x1_ready, mid, -5)
                    dve.tensor_tensor(y[:, mid.slot, :], ctxn[:, mid.slot % 2, :],
                                      one(x_sb[:, bass.ds(mid.n, 1), :]), ALU.add).then_inc(y_ready, 1)
                next(small, None)

            def route(t):
                g = t.slot // GROUP
                wait_groups(dve, score_ready, t, 1)
                dve.tensor_reduce(best[:, :], score_ps, AX, ALU.max).then_inc(best_ready, 1)
                yield
                wait_groups(dve, best_ready, t, 1)
                dve.tensor_tensor(is_best[:, :, :], score_ps, best[:, :, None].to_broadcast([P, GROUP, X]),
                                  ALU.is_equal).then_inc(is_best_ready, 1)
                yield
                wait_groups(dve, is_best_ready, t, 1)
                dve.tensor_tensor(is_best[:, :, :], is_best[:, :, :], falling[:, :, :],
                                  ALU.mult).then_inc(ranked_best, 1)
                yield
                wait_groups(dve, ranked_best, t, 1)
                dve.tensor_reduce(first[:, :], is_best[:, :, :], AX, ALU.max).then_inc(first_ready, 1)
                yield
                wait_groups(dve, first_ready, t, 1)
                dve.tensor_tensor(onehot[:, g, 0:GROUP, :], falling[:, :, :],
                                  first[:, :, None].to_broadcast([P, GROUP, X]),
                                  ALU.is_equal).then_inc(onehot_ready, 1)

            def place(t):
                g = t.slot // GROUP
                wait_groups(dve, rank_ready, t, 1)
                dve.tensor_tensor(at_row[:, :, :], rank_ps, region_start[:, :, :], ALU.add).then_inc(at_row_ready, 1)
                with nc.allow_low_precision(reason="counts up to the number of tiles are exact in bf16"):
                    dve.tensor_reduce(onehot[:, 1 - g, GROUP, :], onehot[:, g].rearrange("p t x -> p x t"),
                                      AX, ALU.add).then_inc(carry_ready, 1)
                yield
                dve.wait_ge(at_row_ready, (t.turn * GROUPS + g) * 2 + 1)
                dve.tensor_tensor(at_row[:, :, :], at_row[:, :, :], onehot[:, g, 0:GROUP, :],
                                  ALU.mult).then_inc(at_row_ready, 1)
                yield
                dve.wait_ge(at_row_ready, (t.turn * GROUPS + g) * 2 + 2)
                with nc.allow_low_precision(reason="row numbers are whole"):
                    dve.tensor_reduce(row_of[:, g, :], at_row[:, :, :], AX, ALU.add).then_inc(row_ready, 1)

            pipelined(dve, BATCHES, queries, after_first=expert_weights)

            steps = [0]

            def done(instruction):
                steps[0] += 1
                instruction.then_inc(table_step, 1)
                dve.wait_ge(table_step, steps[0])

            dve.wait_ge(count_ready, 1)
            dve.wait_ge(prep, 2)
            dve.tensor_tensor(pad_tab[:, :], count_ps, region_start[:, 0, :], ALU.add).then_inc(pads_ready, 1)
            done(dve.tensor_scalar(count_i[:, :], count_ps, float(P - 1), None, ALU.add))
            done(dve.tensor_scalar(tiles_i[:, :], count_i[:, :], P.bit_length() - 1, None, ALU.arith_shift_right))
            done(dve.tensor_copy(tiles_f[:, :], tiles_i[:, :]))
            done(dve.tensor_tensor_scan(tile_end[:, :], ones_x[:, :], tiles_f[:, :], 0.0, ALU.mult, ALU.add))
            done(dve.tensor_scalar(skip_rows[:, :], tiles_f[:, :], float(-P), float(REGION), ALU.mult, ALU.add))
            done(dve.tensor_tensor(past[:, :, :], j_f[:, :, None].to_broadcast([P, TILES_B, X]),
                                   tile_end[:, None, :].to_broadcast([P, TILES_B, X]), ALU.is_ge))
            done(dve.tensor_tensor(skipped[:, :, :], past[:, :, :],
                                   skip_rows[:, None, :].to_broadcast([P, TILES_B, X]), ALU.mult))
            done(dve.tensor_reduce(off_f[:, :], skipped[:, :, :], AX, ALU.add))
            done(dve.tensor_reduce(exp_f[:, :], past[:, :, :], AX, ALU.add))
            done(dve.scalar_tensor_tensor(out=off_f[:, :], in0=j_f[:, :], scalar=float(P), in1=off_f[:, :],
                                          op0=ALU.mult, op1=ALU.add))
            dve.tensor_scalar(row_tab[:, :], off_f[:, :], float(FILL), None, ALU.min).then_inc(table_ready, 1)
            done(dve.tensor_scalar(expert[:, :, :].rearrange("p k i -> p (k i)")[:, MM_LAG:MM_LAG + TILES_B],
                                   exp_f[:, :], float(X - 1), None, ALU.min))
            done(dve.tensor_tensor(packed[:, :, :], expert[:, :, :],
                                   place_value[:, None, :].to_broadcast([P, TURNS_B + 1, BODY]), ALU.mult))
            done(dve.tensor_reduce(packed_f[:, :], packed[:, :, :], AX, ALU.add))
            dve.tensor_copy(expert_tab[:, :], packed_f[:, :]).then_inc(table_ready, 1)
            dve.wait_ge(table_ready, 2)

            packed_experts = []

            def experts(turn, step):
                load_experts(dve, turn, step, packed_experts)
                t = tile_at(turn, TURNS_B, step, MM_LAG)
                if t is not None:
                    wait_tiles(dve, f_ready, t, 1)
                    dve.tensor_tensor(y[:, t.slot, :], f_ps[t.slot % RING], bias_sb[:, expert_columns(packed_experts, step)],
                                      ALU.add).then_inc(f_biased, 1)
                t = tile_at(turn, TURNS_B, step, 7) if step % 2 == 1 else None
                if t is not None:
                    pair = slice(t.slot, t.slot + 2)
                    wait_groups(dve, f_rstd, t, 1, size=2)
                    dve.scalar_tensor_tensor(out=nmr[:, pair], in0=mv[:, pair, 0], scalar=-1.0,
                                             in1=rstd[:, pair], op0=ALU.mult, op1=ALU.mult).then_inc(f_nmr, 1)
                t = tile_at(turn, TURNS_B, step, 4)
                if t is not None:
                    wait_tiles(dve, f_biased, t, 1)
                    dve.bn_stats(stats[:, t.slot, :], y[:, t.slot, :]).then_inc(f_stats, 1)
                t = tile_at(turn, TURNS_B, step, 5) if step % 2 == 1 else None
                if t is not None:
                    wait_tiles(dve, f_stats, t, 2)
                    held(dve, t.turn, dve_passed)
                    for i in range(2):
                        last = dve.bn_aggr(mv[:, t.slot + i, :], stats[:, t.slot + i, :])
                    last.then_inc(f_mv, 1)

            pipelined(dve, TURNS_B, experts)

        @block.tensor
        def _(pe):
            def fold(i, loaded):
                pe.wait_ge(loaded, 64)
                for c in range(2):
                    for m in range(2):
                        last = pe.matmul(fold_ps[:, c * E:(c + 1) * E], w_raw[:, 2 * i, m, c * P:(c + 1) * P],
                                         w_raw[:, 2 * i + 1, m, :], start=(m == 0), stop=(m == 1))
                last.then_inc(fold_ready, 1)
                pe.wait_ge(b_widened, i + 1)
                for m in range(2):
                    last = pe.matmul(fold_row_ps, b_wide[:, i, m, :], w_raw[:, 2 * i + 1, m, :],
                                     start=(m == 0), stop=(m == 1))
                last.then_inc(fold_ready, 1)

            def keep_warm(count):
                for _ in range(count):
                    pe.matmul(bank[2][:, :], ones[:, :], ones[:, None, :].to_broadcast([P, 4, P]),
                              start=True, stop=True)

            pe.wait_ge(ones_ready, 1)
            keep_warm(9)
            fold(0, wk_loaded)
            pe.wait_ge(fold_saved, 1)

            def project(t, weights, done):
                for c in range(2):
                    last = pe.matmul(proj_ps[t.slot % 2],
                                     xT_sb[:, t.slot // GROUP, c, (t.slot % GROUP) * P:(t.slot % GROUP + 1) * P],
                                     weights[:, c, :], start=(c == 0), stop=(c == 1))
                last.then_inc(done, 1)

            def keys(turn, step):
                t = tile_at(turn, BATCHES, step, 2)
                if t is not None:
                    par = t.slot % 2
                    wait_tiles(pe, xTs_ready, t, 1)
                    wait_tiles(pe, k_neg, t, -1)
                    for xi, wi in ((0, 0), (0, 1), (1, 0)):
                        for c in range(2):
                            last = pe.matmul(proj_ps[par], xTs[:, t.slot % GROUP, xi, c, :], wkc[:, wi, c, :],
                                             start=(xi + wi + c == 0), stop=((xi, c) == (1, 1)))
                    last.then_inc(k_ready, 1)
                for lag, at_slots in ((5, (0,)), (4, range(1, BODY))):
                    t = tile_at(turn, BATCHES, step, lag)
                    if t is None or t.slot not in at_slots:
                        continue
                    wait_tiles(pe, xr_ready, t, 1)
                    if t.slot == 0:
                        for h in range(2):
                            wait_turns(pe, g_saved[h], t, 0)
                    for h in range(2):
                        last = pe.matmul(g_ps[h], e_sb[:, t.slot % GROUP, h * P:(h + 1) * P],
                                         xr[:, t.slot % GROUP, :],
                                         start=(t.slot == 0), stop=(t.slot == BODY - 1))
                    last.then_inc(g_done, 1)
                t = tile_at(turn, BATCHES, step, 7)
                if t is not None and t.slot == BODY - 1:
                    for c in range(2):
                        wait_turns(pe, gT_saved[c], t, 1)
                    pe.wait_ge(wv_loaded, 32)
                    for h in range(2):
                        for c in range(2):
                            last = pe.matmul(kv_ps[:, h, :], gT_sb[:, c, h * P:(h + 1) * P],
                                             wvT_sb[:, c, h * P:(h + 1) * P], start=(c == 0), stop=(c == 1))
                    last.then_inc(kv_ready, 1)
                t = tile_at(turn, BATCHES, step, 6)
                if t is not None and t.slot == BODY - 1:
                    pe.wait_ge(fold_saved, 4)
                    for h in range(2):
                        wait_turns(pe, g_saved[h], t, 1)
                    for c in range(2):
                        for h in range(2):
                            last = pe.transpose(gT_ps[c][:, h * P:(h + 1) * P], g_sb[:, h, c * P:(c + 1) * P],
                                                ident[:, :])
                    last.then_inc(gT_ready, 1)

            def queries_weights():
                fold(1, wq_loaded)

            pe.wait_ge(consts_v, 5)
            pipelined(pe, BATCHES, keys, after_first=queries_weights, drain=False)
            keys(BATCHES, 0)
            keys(BATCHES, 1)

            pe.wait_ge(k_neg, NT)
            pe.wait_ge(sign_ready, 1)

            def transpose_pair(turn, step, lags):
                for lag in lags:
                    t = tile_at(turn, BATCHES, step, lag)
                    if t is None:
                        continue
                    wait_tiles(pe, x1_ready, t, 1)
                    if t.slot % 2 == 0:
                        wait_groups(pe, x1T_saved, t, 0, size=2)
                    for c in range(2):
                        last = pe.transpose(x1T_ps[:, t.slot % 2, c, :], x1[:, t.slot, c * P:(c + 1) * P],
                                            ident[:, :])
                    last.then_inc(x1T_ready, 1)

            def score_pair(turn, step, lags):
                for lag in lags:
                    t = tile_at(turn, BATCHES, step, lag)
                    if t is None:
                        continue
                    i = t.slot % GROUP
                    wait_groups(pe, x1T_saved, t, 1, size=2)
                    for c in range(2):
                        last = pe.matmul(score_ps[:, i, :], x1T[:, i, c, :], sign[:, c, :],
                                         start=(c == 0), stop=(c == 1))
                    if i == GROUP - 1:
                        last.then_inc(score_ready, 1)

            def queries(turn, step):
                if isinstance(turn, int) and turn == 0:
                    if step + 2 < BODY:
                        keys(BATCHES, step + 2)
                t = tile_at(turn, BATCHES, step, 3)
                if t is not None:
                    par = t.slot % 2
                    wait_tiles(pe, eT_saved, t, 1)
                    wait_tiles(pe, ctxn_ready, t, -1)
                    if t.slot == 0:
                        pe.wait_ge(kvd_ready, 4 * (t.turn + 1))
                    for h in range(2):
                        last = pe.matmul(ctx_ps[par][:, h, :], eT_sb[:, par, h, :],
                                         one(kvd[:, bass.ds(t.turn, 1), h, :]), start=True, stop=True)
                    last.then_inc(ctx_ready, 1)
                t = tile_at(turn, BATCHES, step, 2)
                if t is not None:
                    par = t.slot % 2
                    wait_tiles(pe, eq_ready, t, 1)
                    wait_tiles(pe, eT_saved, t, 0)
                    for c in range(2):
                        last = pe.transpose(eT_ps[:, c, :], e_sb[:, t.slot % GROUP, c * P:(c + 1) * P], ident[:, :])
                    last.then_inc(eT_ready, 1)
                if step % 2 == 1:
                    transpose_pair(turn, step, (7, 6))
                t = tile_at(turn, BATCHES, step, 0)
                if t is not None:
                    if t.slot % GROUP == 0:
                        wait_turns(pe, xT_loaded[t.slot // GROUP], t, 1 + BATCHES, 16)
                    wait_tiles(pe, q_neg, t, -1)
                    project(t, wqc, q_ready)
                if step % 2 == 0:
                    score_pair(turn, step, (8, 7))
                if step % GROUP == 3:
                    t = tile_at(turn, BATCHES, step, 11)
                    if t is not None:
                        g = t.slot // GROUP
                        wait_groups(pe, onehot_ready, t, 1)
                        pe.matmul(rank_ps, before[:, :], onehot[:, g, 0:GROUP, :], start=True, stop=False)
                        for i in range(GROUP - 1):
                            pe.matmul(rank_ps[:, i + 1:GROUP, :], ones[:, :],
                                      onehot[:, g, i:i + 1, :].to_broadcast([P, GROUP - 1 - i, X]),
                                      start=False, stop=False)
                        pe.matmul(rank_ps, ones[:, :],
                                  onehot[:, g, GROUP:GROUP + 1, :].to_broadcast([P, GROUP, X]),
                                  start=False, stop=True).then_inc(rank_ready, 1)

            pipelined(pe, BATCHES, queries)

            pe.wait_ge(carry_ready, BATCHES * GROUPS)
            pe.matmul(count_ps, ones[:, :], onehot[:, 0, GROUP, :], start=True, stop=True).then_inc(count_ready, 1)
            pe.wait_ge(table_ready, 2)
            pe.wait_ge(w_ready, 2)
            pe.wait_ge(row_stored[GROUP], 16 * BATCHES)
            keep_warm(13)

            packed_experts = []

            def experts(turn, step):
                load_experts(pe, turn, step, packed_experts)
                t = tile_at(turn, TURNS_B, step, 0)
                if t is not None:
                    r = t.slot % RING
                    wait_turns(pe, xs_loaded[t.slot], t, 1, 16)
                    wait_tiles(pe, xsT_saved, t, 1 - RING)
                    for c in range(2):
                        last = pe.transpose(xsT_ps[r][:, c, :], xs[:, t.slot, c * P:(c + 1) * P], ident[:, :])
                    last.then_inc(xsT_ready, 1)
                t = tile_at(turn, TURNS_B, step, MM_LAG)
                if t is not None:
                    r = t.slot % RING
                    wait_tiles(pe, xsT_saved, t, 1)
                    wait_tiles(pe, f_biased, t, 1 - RING)
                    for c in range(2):
                        last = pe.matmul(f_ps[r], xsT[:, r, c, :], w_sb[:, c, expert_columns(packed_experts, step)],
                                         start=(c == 0), stop=(c == 1))
                    last.then_inc(f_ready, 1)

            pipelined(pe, TURNS_B, experts)


def kernel(**inputs):
    import numpy as np
    import concourse.bacc as bacc
    from concourse.bass_utils import run_bass_kernel_spmd

    a = {k.split("_", 2)[2]: np.asarray(v) for k, v in inputs.items()}
    B, S, E = a["hidden_states"].shape
    flat = a["hidden_states"].reshape(B * S, E)
    laid = {
        "x": flat, "xT": flat.T,
        "Wq": a["Wq"], "Wk": a["Wk"],
        "WfqT": a["Wfq"].T, "WfkT": a["Wfk"].T,
        "WvT": a["Wv"].T,
        "bq": a["bq"].reshape(2, P).T, "bk": a["bk"].reshape(2, P).T, "bv": a["bv"], "bfq": a["bfq"], "bfk": a["bfk"],
        "sigsT": a["tile_sigs"].T, "W": a["W"], "b": a["b"],
    }
    laid = {k: np.ascontiguousarray(v) for k, v in laid.items()}
    nc = bacc.Bacc("TRN2", target_bir_lowering=False, num_devices=1)
    aps = {k: nc.dram_tensor(f"in_{k}", v.shape, mybir.dt.from_np(v.dtype), kind="ExternalInput").ap()
           for k, v in laid.items()}
    out = nc.dram_tensor("out", (B * S, E), F32, kind="ExternalOutput").ap()
    build(nc, out=out, **aps)
    r = run_bass_kernel_spmd(nc, [{f"in_{k}": v for k, v in laid.items()}], core_ids=[0])
    return r.results[0]["out"].reshape(B, S, E)
```
